# Optimizing a Trainium2 kernel written in Bass

```python
import numpy as np
import jax
import jax.numpy as jnp

def _softmax(x, axis=-1):
    return jax.nn.softmax(x, axis=axis)

def _gelu(x):
    return jax.nn.gelu(x, approximate=True)

def _silu(x):
    return jax.nn.silu(x)

def _sigmoid(x):
    return jax.nn.sigmoid(x)

def _layernorm(x, axis=-1, eps=1e-05):
    m = jnp.mean(x, axis=axis, keepdims=True)
    v = jnp.var(x, axis=axis, keepdims=True)
    return (x - m) / jnp.sqrt(v + eps)

def _scatter_add(tgt, idx, src, axis=0):
    return tgt.at[idx].add(src)

def _segment_sum(src, seg, n):
    return jax.ops.segment_sum(src, seg, n)
kernel_name = 'mk_adaln_d1_jaxref_r8_332c52'

def setup_inputs(seed: int=0):
    np.random.seed(seed)
    _w = jnp.asarray

    def _L0_attn_setup():
        import jax, jax.numpy as jnp
        import numpy as np
        import math
        EMB = 256
        HEADS = 16
        HEAD_DIM = EMB // HEADS
        SCALE = math.sqrt(HEAD_DIM)

        def srms_norm(x, eps_min=1e-12):
            d = x.shape[-1]
            xf = x.astype(jnp.float32)
            norm = jnp.linalg.norm(xf * (1.0 / math.sqrt(d)), axis=-1, keepdims=True)
            norm = jnp.maximum(norm, eps_min)
            return (xf / norm).astype(x.dtype)
        key = jax.random.key(seed)
        ks = jax.random.split(key, 6)
        x = jax.random.normal(ks[0], (4, 512, EMB), dtype=jnp.float32)
        std = 1.0 / math.sqrt(EMB)
        Wq = jax.random.normal(ks[1], (EMB, EMB), dtype=jnp.float32) * std
        Wk = jax.random.normal(ks[2], (EMB, EMB), dtype=jnp.float32) * std
        Wv = jax.random.normal(ks[3], (EMB, EMB), dtype=jnp.float32) * std
        Wu = jax.random.normal(ks[4], (EMB, EMB), dtype=jnp.float32) * std
        Wo = jax.random.normal(ks[5], (EMB, EMB), dtype=jnp.float32) * std
        return {'x': x, 'Wq': Wq, 'Wk': Wk, 'Wv': Wv, 'Wu': Wu, 'Wo': Wo}
    _L0_attn_in = _L0_attn_setup()

    def _L0_ffn_setup():
        import jax, jax.numpy as jnp
        import numpy as np
        H = 256
        F = 704
        E = 8
        TOP_K = 2
        N_SHARED = 1
        SCALE = 0.02

        def _ffn(x, wg, wu, wd):
            return jax.nn.silu(x @ wu) * (x @ wg) @ wd
        key = jax.random.key(seed)
        ks = jax.random.split(key, 9)
        inp = {'hidden_state': jax.random.normal(ks[0], (2, 128, H), dtype=jnp.float32), 'gate_w': jax.random.normal(ks[1], (E, H), dtype=jnp.float32) * SCALE, 'w_gate': jax.random.normal(ks[2], (E, H, F), dtype=jnp.float32) * SCALE, 'w_up': jax.random.normal(ks[3], (E, H, F), dtype=jnp.float32) * SCALE, 'w_down': jax.random.normal(ks[4], (E, F, H), dtype=jnp.float32) * SCALE, 'sw_gate': jax.random.normal(ks[5], (N_SHARED, H, F), dtype=jnp.float32) * SCALE, 'sw_up': jax.random.normal(ks[6], (N_SHARED, H, F), dtype=jnp.float32) * SCALE, 'sw_down': jax.random.normal(ks[7], (N_SHARED, F, H), dtype=jnp.float32) * SCALE}
        return inp
    _L0_ffn_in = _L0_ffn_setup()
    _L0_c = _w((lambda *s: np.random.randn(*s).astype(np.float32) * 0.05)(4, 256))
    _L0_wmod = _w((lambda *s: np.random.randn(*s).astype(np.float32) * 0.05)(256, 6 * 256) * 256 ** (-0.5))
    _d = {'L0_attn_x': _L0_attn_in['x'], 'L0_attn_Wq': _L0_attn_in['Wq'], 'L0_attn_Wk': _L0_attn_in['Wk'], 'L0_attn_Wv': _L0_attn_in['Wv'], 'L0_attn_Wu': _L0_attn_in['Wu'], 'L0_attn_Wo': _L0_attn_in['Wo'], 'L0_ffn_gate_w': _L0_ffn_in['gate_w'], 'L0_ffn_w_gate': _L0_ffn_in['w_gate'], 'L0_ffn_w_up': _L0_ffn_in['w_up'], 'L0_ffn_w_down': _L0_ffn_in['w_down'], 'L0_ffn_sw_gate': _L0_ffn_in['sw_gate'], 'L0_ffn_sw_up': _L0_ffn_in['sw_up'], 'L0_ffn_sw_down': _L0_ffn_in['sw_down'], 'L0_c': _L0_c, 'L0_wmod': _L0_wmod}
    _x0 = _d['L0_attn_x']
    _d['L0_attn_x'] = jax.random.normal(jax.random.fold_in(jax.random.key(seed), 1), (4, 256, 256), dtype=_x0.dtype)
    del _x0
    return _d

def reference(L0_attn_x, L0_attn_Wq, L0_attn_Wk, L0_attn_Wv, L0_attn_Wu, L0_attn_Wo, L0_ffn_gate_w, L0_ffn_w_gate, L0_ffn_w_up, L0_ffn_w_down, L0_ffn_sw_gate, L0_ffn_sw_up, L0_ffn_sw_down, L0_c, L0_wmod):

    def _L0_attn_ref(x, Wq, Wk, Wv, Wu, Wo):
        import jax, jax.numpy as jnp
        import numpy as np
        import math
        EMB = 256
        HEADS = 16
        HEAD_DIM = EMB // HEADS
        SCALE = math.sqrt(HEAD_DIM)

        def srms_norm(x, eps_min=1e-12):
            d = x.shape[-1]
            xf = x.astype(jnp.float32)
            norm = jnp.linalg.norm(xf * (1.0 / math.sqrt(d)), axis=-1, keepdims=True)
            norm = jnp.maximum(norm, eps_min)
            return (xf / norm).astype(x.dtype)
        B, L, D = x.shape
        H, dh = (HEADS, HEAD_DIM)
        q = (x @ Wq).reshape(B, L, H, dh).transpose(0, 2, 1, 3)
        k = (x @ Wk).reshape(B, L, H, dh).transpose(0, 2, 1, 3)
        v = (x @ Wv).reshape(B, L, H, dh).transpose(0, 2, 1, 3)
        u = (x @ Wu).reshape(B, L, H, dh).transpose(0, 2, 1, 3)
        q = jax.nn.relu(q) / SCALE
        k = jax.nn.relu(k) / SCALE
        u = jax.nn.silu(u)
        kv = jnp.einsum('bhlk,bhlv->bhkv', k, v)
        out = jnp.einsum('bhlk,bhkv->bhlv', q, kv)
        out = srms_norm(out) * u
        out = out.transpose(0, 2, 1, 3).reshape(B, L, D)
        return out @ Wo

    def _L0_ffn_ref(hidden_state, gate_w, w_gate, w_up, w_down, sw_gate, sw_up, sw_down):
        import jax, jax.numpy as jnp
        import numpy as np
        H = 256
        F = 704
        E = 8
        TOP_K = 2
        N_SHARED = 1
        SCALE = 0.02

        def _ffn(x, wg, wu, wd):
            return jax.nn.silu(x @ wu) * (x @ wg) @ wd
        B, S, Hd = hidden_state.shape
        x = hidden_state.reshape(-1, Hd)
        T = x.shape[0]
        logits = x @ gate_w.T
        score = jax.nn.softmax(logits, axis=-1)
        topk_w, topk_i = jax.lax.top_k(score, TOP_K)
        topk_w = topk_w / (jnp.sum(topk_w, axis=-1, keepdims=True) + 1e-20)
        dense_w = jnp.zeros((T, E), dtype=x.dtype).at[jnp.arange(T)[:, None], topk_i].add(topk_w)
        expert_out = jax.vmap(lambda wg, wu, wd: _ffn(x, wg, wu, wd))(w_gate, w_up, w_down)
        y = jnp.einsum('te,eth->th', dense_w, expert_out)
        for i in range(sw_gate.shape[0]):
            y = y + _ffn(x, sw_gate[i], sw_up[i], sw_down[i])
        return y.reshape(B, S, Hd)
    x = L0_attn_x
    mod = (_silu(L0_c) @ L0_wmod).reshape(L0_c.shape[0], 6, 1, -1)
    sa, ca, ga, sb, cb, gb = (mod[:, 0], mod[:, 1], mod[:, 2], mod[:, 3], mod[:, 4], mod[:, 5])
    ga = (2 * (ga >= 0) - 1) * jnp.maximum(jnp.abs(ga), 0.25)
    gb = (2 * (gb >= 0) - 1) * jnp.maximum(jnp.abs(gb), 0.25)
    h = _layernorm(x, axis=-1) * (1 + ca) + sa
    x = x + ga * _L0_attn_ref(h, L0_attn_Wq, L0_attn_Wk, L0_attn_Wv, L0_attn_Wu, L0_attn_Wo)
    h = _layernorm(x, axis=-1) * (1 + cb) + sb
    x = x + gb * _L0_ffn_ref(h, L0_ffn_gate_w, L0_ffn_w_gate, L0_ffn_w_up, L0_ffn_w_down, L0_ffn_sw_gate, L0_ffn_sw_up, L0_ffn_sw_down)
    return x

_drawn_inputs = setup_inputs


def setup_inputs(seed=0):
    import zlib

    import numpy as np

    out = dict(_drawn_inputs(seed))
    spreads = {}
    factors = {'L0_ffn_gate_w': 8.0,
     'L0_ffn_w_gate': 8.0,
     'L0_ffn_w_up': 8.0,
     'L0_ffn_w_down': 8.0,
     'L0_ffn_sw_gate': 8.0,
     'L0_ffn_sw_up': 8.0,
     'L0_ffn_sw_down': 8.0}
    for name, (base, spread) in spreads.items():
        noise = np.random.default_rng([zlib.crc32(name.encode()), seed]).standard_normal(out[name].shape)
        drawn = base * np.exp(spread * noise) if base else spread * noise
        out[name] = jnp.asarray(drawn.astype(out[name].dtype))
    for name, factor in factors.items():
        out[name] = (out[name] * factor).astype(out[name].dtype)
    return out
```

```python
import concourse.bass as bass
from concourse import mybir
from contextlib import ExitStack


def adaln_block(nc, x, wq, wk, wv, wu, wo, gate_w, w_gate, w_up, w_down, sw_gate, sw_up, sw_down, c, wmod, out):
    f32 = mybir.dt.float32
    f32r = mybir.dt.float32r
    ALU = mybir.AluOpType
    ACT = mybir.ActivationFunctionType
    AX = mybir.AxisListType

    P = 128
    B, L, D = x.shape
    T = B * L // P
    TB = L // P
    KD = D // P
    HD = 16
    NH = D // HD
    E, _, F = w_gate.shape
    NX = E + 1
    FH = F // 2
    GU = KD * 2 * F
    FC = 6
    FR = [128, 128, 128, 128, 96, 96]
    FO = [0, 128, 256, 384, 512, 608]
    W1 = GU + FC * D
    EPS = 1e-5

    ctx = ExitStack()
    with ctx:
        def sb(name, shape, dt=f32):
            return ctx.enter_context(nc.sbuf_tensor(name, shape, dt))

        def sem(name):
            return ctx.enter_context(nc.semaphore(name))

        ident = sb("ident", [P, P])
        blockmask = sb("blockmask", [P, P])
        sel = sb("sel", [B, B, P])
        eps = sb("eps", [P, 1])
        prio = sb("prio", [P, T, E])
        c_sb = sb("c_sb", [B, D])
        sc_sb = sb("sc_sb", [B, D])
        scT = sb("scT", [P, KD, B])
        modT = sb("modT", [P, 4, B])
        modrow = sb("modrow", [B, 4, D])
        modB = sb("modB", [P, B, 4, D])
        gw_sb = sb("gw_sb", [E, D])
        gwT = sb("gwT", [P, KD, E])
        wqkvu = sb("wqkvu", [P, KD, 4, D])
        wo_sb = sb("wo_sb", [P, KD, D])
        x_sb = sb("x_sb", [P, T, D])
        xn = sb("xn", [P, T, D])
        hT = sb("hT", [P, KD, T * P])
        kvm = sb("kvm", [P, B, KD, P])
        ou = sb("ou", [P, T, D])
        stats = sb("stats", [P, T, 6])
        mv = sb("mv", [P, T, 2])
        rstd = sb("rstd", [P, T])
        hn = sb("hn", [P, T, NH])
        hr = sb("hr", [P, T, NH])
        lg = sb("lg", [P, 8, T, E])
        sm = sb("sm", [P, 8, T])
        dw = sb("dw", [P, T, E])
        raw = sb("raw", [P, 1, W1])
        whi = sb("whi", [P, 2, W1], f32r)
        wlo = sb("wlo", [P, 2, W1], f32r)
        aT = hT
        y = ou
        def front(name, shape):
            return attn.enter_context(nc.sbuf_tensor(name, shape, f32))
        attn = ExitStack()
        wmod_sb = front("wmod_sb", [P, KD, 6 * D])
        kvu = front("kvu", [P, T, 3, D])
        qT = front("qT", [P, KD, T * P])
        mtmp = kvu[0:B, 0:4].rearrange("b t w d -> b (t w d)").rearrange("b (r w d) -> b r w d", r=3, w=4)
        sq = wmod_sb[:, 0, 0:2 * TB * D].rearrange("p (i d) -> p i d", i=2)
        attn.close()
        hThi = sb("hThi", [P, KD, T * P], f32r)
        hTlo = sb("hTlo", [P, KD, T * P], f32r)
        sil = sb("sil", [P, 2, FH])
        actv = sb("actv", [P, 2, F])
        aThi = sb("aThi", [P, FC, P], f32r)
        aTlo = sb("aTlo", [P, FC, P], f32r)

        bank = [ctx.enter_context(nc.psum_tensor(f"bank{i}", [P, 512], f32)) for i in range(8)]

        names = ("d_c d_gw d_wmod d_wqkvu d_wo d_out const silc cT scT_ok gwT_ps gwT_ok modT_ps modT_ok modrow_ps "
                 "modrow_ok mv_ok std_ok xn_ok xT_ps hT_a hT_v qT_ps qT_a qT_v kvu_ps kvu_v kvu_a kv_ps kvm_ok o_ps sq_ok "
                 "ou_ok hn_sum hn_sqrt a_ok modB_ps modB_ok aT_ps aT_a aT_v wo_ps x2_ok mv2_ok std2_ok xn2_ok h2_ok "
                 "h2T_ps h2hi h2lo lgT_ok lg_ps ex_in ex_ok dw_ok dch ach pch split gu_ps silu_ok mul_ok t_ps thi tlo "
                 "y_ps y_ok raw_used").split()
        s = {n: sem(n) for n in names}
        d_x = [sem(f"d_x{b}") for b in range(B)]
        d_raw = [sem(f"d_raw{i}") for i in range(2)]

        raw_gu = raw[:, :, 0:GU].rearrange("p s (k w f) -> p s k w f", k=KD, w=2)
        raw_d = raw[:, :, GU:W1].rearrange("p s (c d) -> p s c d", c=FC)
        hi_gu = whi[:, :, 0:GU].rearrange("p s (k w f) -> p s k w f", k=KD, w=2)
        lo_gu = wlo[:, :, 0:GU].rearrange("p s (k w f) -> p s k w f", k=KD, w=2)
        hi_d = whi[:, :, GU:W1].rearrange("p s (c d) -> p s c d", c=FC)
        lo_d = wlo[:, :, GU:W1].rearrange("p s (c d) -> p s c d", c=FC)
        GATE, UP = 0, 1

        block = ctx.enter_context(nc.Block())

        @block.sync
        def _(sp):
            sp.dma_start(c_sb[:], c).then_inc(s["d_c"], 16)
            for b in range(B):
                sp.dma_start(x_sb[:, TB * b:TB * b + TB, :], x[b].rearrange("(t p) d -> p t d", p=P)).then_inc(d_x[b], 16)
            sp.dma_start(wmod_sb[:], wmod.rearrange("(k p) n -> p k n", p=P)).then_inc(s["d_wmod"], 16)
            sp.dma_start(gw_sb[:], gate_w).then_inc(s["d_gw"], 16)
            for i, w in enumerate((wq, wk, wv, wu)):
                sp.dma_start(wqkvu[:, :, i, :], w.rearrange("(k p) n -> p k n", p=P)).then_inc(s["d_wqkvu"], 16)
            sp.dma_start(wo_sb[:], wo.rearrange("(k p) n -> p k n", p=P)).then_inc(s["d_wo"], 16)
            for n in range(NX):
                g, u, d = (sw_gate[0], sw_up[0], sw_down[0]) if n == 0 else (w_gate[n - 1], w_up[n - 1], w_down[n - 1])
                sl = 0
                if n >= 1:
                    sp.wait_ge(s["raw_used"], n)
                else:
                    sp.wait_ge(s["pch"], 1)
                sp.dma_start(raw_gu[:, sl, :, GATE, :], g.rearrange("(k p) f -> p k f", p=P)).then_inc(d_raw[n % 2], 16)
                sp.dma_start(raw_gu[:, sl, :, UP, :], u.rearrange("(k p) f -> p k f", p=P)).then_inc(d_raw[n % 2], 16)
                sp.dma_start(raw_d[:, sl, 0:4, :], d[0:512].rearrange("(c p) d -> p c d", p=P)).then_inc(d_raw[n % 2], 16)
                sp.dma_start(raw_d[0:96, sl, 4:6, :], d[512:704].rearrange("(c p) d -> p c d", p=96)).then_inc(d_raw[n % 2], 16)
            ov = out.rearrange("b (t p) d -> p (b t) d", p=P)
            for t in range(T):
                sp.wait_ge(s["y_ok"], (NX - 1) * T + t + 1 + T)
                sp.dma_start(ov[:, t, :], y[:, t, :]).then_inc(s["d_out"], 16)
            sp.wait_ge(s["d_out"], 16 * T)

        @block.gpsimd
        def _(pool):
            chain = [0]

            def link(ins):
                chain[0] += 1
                ins.then_inc(s["pch"], 1)
                pool.wait_ge(s["pch"], chain[0])
            link(pool.memset(raw[96:128, :, GU + 4 * D:W1], 0.0))
            link(pool.memset(ident[:], 1.0))
            pool.affine_select(out=ident[:], in_=ident[:], compare_op=ALU.is_equal, fill=0.0, base=0,
                               pattern=[[-1, P]], channel_multiplier=1).then_inc(s["const"], 1)
            pool.memset(eps[:], EPS).then_inc(s["const"], 1)
            link(pool.memset(sel[:], 1.0))
            pool.affine_select(out=sel[:], in_=sel[:], compare_op=ALU.is_equal, fill=0.0, base=0,
                               pattern=[[-1, B], [0, P]], channel_multiplier=1).then_inc(s["const"], 1)
            link(pool.memset(blockmask[:], 1.0))
            bm = blockmask[:].rearrange("p (j i) -> p j i", i=HD)
            link(pool.affine_select(out=bm, in_=bm, compare_op=ALU.is_ge, fill=0.0, base=0,
                                    pattern=[[-HD, P // HD], [0, HD]], channel_multiplier=1))
            pool.affine_select(out=bm, in_=bm, compare_op=ALU.is_ge, fill=0.0, base=HD - 1,
                               pattern=[[HD, P // HD], [0, HD]], channel_multiplier=-1).then_inc(s["const"], 1)
            pool.iota(prio[:], pattern=[[0, T], [-1, E]], base=E, channel_multiplier=0,
                      allow_small_or_imprecise_dtypes=True).then_inc(s["const"], 1)
            for n in range(NX):
                pool.wait_ge(d_raw[n % 2], 64 * (n // 2 + 1))
                if n >= 2:
                    pool.wait_ge(s["y_ps"], T * (n - 1))
                link(pool.tensor_scalar(whi[:, n % 2, :], raw[:, 0, :], 1.0, 0.0, ALU.mult, ALU.add))
                pool.tensor_tensor(wlo[:, n % 2, :], raw[:, 0, :], whi[:, n % 2, :].bitcast(f32), ALU.subtract
                                   ).then_inc(s["split"], 1)
                pool.wait_ge(s["split"], n + 1)
                pool.sem_inc(s["raw_used"], 1)

        @block.scalar
        def _(act_e):
            a = act_e
            a.wait_ge(s["d_c"], 16)
            a.activation(sc_sb[:], c_sb[:], ACT.Silu).then_inc(s["silc"], 1)
            a.wait_ge(s["const"], 5)
            a.wait_ge(s["mv_ok"], T)
            a.activation(rstd[:], mv[:, :, 1], ACT.Sqrt, bias=eps[:]).then_inc(s["std_ok"], 1)
            a.wait_ge(s["modT_ok"], 2)
            for b in range(0, B, 2):
                a.wait_ge(s["xT_ps"], b + 1)
                for k in range(KD):
                    a.activation(hT[:, k, b * L:(b + 1) * L], bank[4 + b][:, k * L:(k + 1) * L], ACT.Identity,
                                 scale=modT[:, 2 + k, b:b + 1], bias=modT[:, k, b:b + 1]).then_inc(s["hT_a"], 1)
            for i in (0, 2):
                a.wait_ge(s["qT_ps"], i + 1)
                a.activation(qT[:, i // 2, (i % 2) * 512:(i % 2) * 512 + 512], bank[i][:], ACT.Relu, scale=0.25
                             ).then_inc(s["qT_a"], 1)
            for t in range(T):
                a.wait_ge(s["kvu_ps"], t + 1)
                a.activation(kvu[:, t, 2, :], bank[5 + 2 * (t % 2)][:, 0:D], ACT.Silu).then_inc(s["kvu_a"], 1)
            for b in range(B):
                a.wait_ge(s["o_ps"], b + 1)
                if b >= 2:
                    a.wait_ge(s["hn_sum"], b - 1)
                a.activation(sq[:, b % 2, :], bank[4 + b][:], ACT.Square).then_inc(s["sq_ok"], 1)
            for i in range(2 * B):
                a.wait_ge(s["modB_ps"], i + 1)
                b, h = i // 2, i % 2
                a.activation(modB[:, b, 2 * h:2 * h + 2, :].rearrange("p w d -> p (w d)"), bank[i % 4][:], ACT.Copy
                             ).then_inc(s["modB_ok"], 1)
            a.wait_ge(s["hn_sum"], B)
            a.activation(hn[:], hn[:], ACT.Sqrt, scale=1.0 / HD).then_inc(s["hn_sqrt"], 1)
            for b in range(0, B, 2):
                a.wait_ge(s["aT_ps"], b + 1)
                a.activation(aT[:, :, b * L:(b + 1) * L], bank[4 + b][:].rearrange("p (k t) -> p k t", k=KD), ACT.Copy
                             ).then_inc(s["aT_a"], 1)
            a.wait_ge(s["mv2_ok"], T)
            a.activation(rstd[:], mv[:, :, 1], ACT.Sqrt, bias=eps[:]).then_inc(s["std2_ok"], 1)
            for b in range(B):
                a.wait_ge(s["h2T_ps"], b + 1)
                a.activation(hThi[:, :, b * L:(b + 1) * L], bank[4 + b][:].rearrange("p (k t) -> p k t", k=KD), ACT.Copy
                             ).then_inc(s["h2hi"], 1)
            a.wait_ge(s["ex_in"], 1)
            a.activation(lg[:, 1], lg[:, 0], ACT.Exp).then_inc(s["ex_ok"], 1)
            for st in range(NX * T):
                for q in range(2):
                    a.wait_ge(s["gu_ps"], 2 * st + q + 1)
                    a.activation(sil[:, q, :], bank[2 * q + 1][:, 0:FH], ACT.Silu).then_inc(s["silu_ok"], 1)
                a.wait_ge(s["t_ps"], st + 1)
                a.activation(aThi[:, 0:4, :], bank[4][:], ACT.Copy).then_inc(s["thi"], 1)
                a.activation(aThi[0:96, 4:6, :], bank[5][0:96, 0:256], ACT.Copy).then_inc(s["thi"], 1)

        @block.vector
        def _(v):
            chain = [0]

            def link(ins):
                chain[0] += 1
                ins.then_inc(s["dch"], 1)
                v.wait_ge(s["dch"], chain[0])

            def norm_stats(src, ok):
                for t in range(T):
                    v.bn_stats(stats[:, t, :], src[:, t, :]).then_inc(s["dch"], 1)
                    chain[0] += 1
                v.wait_ge(s["dch"], chain[0])
                for t in range(T):
                    v.bn_aggr(mv[:, t, :], stats[:, t, :]).then_inc(s[ok], 1)

            for b in range(B):
                v.wait_ge(d_x[b], 16)
            norm_stats(x_sb, "mv_ok")
            v.wait_ge(s["std_ok"], 1)
            link(v.reciprocal(rstd[:], rstd[:]))
            for t in range(T):
                v.tensor_scalar(xn[:, t, :], x_sb[:, t, :], mv[:, t, 0:1], rstd[:, t:t + 1], ALU.subtract, ALU.mult
                                ).then_inc(s["xn_ok"], 1)
            v.wait_ge(s["cT"], 1)
            v.tensor_copy(scT[:], bank[0][:, 0:KD * B].rearrange("p (k b) -> p k b", k=KD)).then_inc(s["scT_ok"], 1)
            v.wait_ge(s["gwT_ps"], 1)
            v.tensor_copy(gwT[:], bank[1][:, 0:KD * E].rearrange("p (k e) -> p k e", k=KD)).then_inc(s["gwT_ok"], 1)
            v.wait_ge(s["modT_ps"], 1)
            v.tensor_copy(modT[:, 0:2, :], bank[2][:, 0:2 * B].rearrange("p (k b) -> p k b", b=B)).then_inc(s["modT_ok"], 1)
            v.tensor_scalar(modT[:, 2:4, :], bank[2][:, 2 * B:4 * B].rearrange("p (k b) -> p k b", b=B), 1.0, None, ALU.add
                            ).then_inc(s["modT_ok"], 1)
            v.wait_ge(s["modT_ok"], 2)
            for b in range(1, B, 2):
                v.wait_ge(s["xT_ps"], b + 1)
                for k in range(KD):
                    v.tensor_scalar(hT[:, k, b * L:(b + 1) * L], bank[4 + b][:, k * L:(k + 1) * L],
                                    modT[:, 2 + k, b:b + 1], modT[:, k, b:b + 1], ALU.mult, ALU.add).then_inc(s["hT_v"], 1)
            v.wait_ge(s["modrow_ps"], 1)
            link(v.tensor_copy(mtmp[:, 0, 0:2, :].rearrange("b w d -> b (w d)"), bank[3][0:B, :]))
            v.wait_ge(s["modrow_ps"], 2)
            link(v.tensor_copy(mtmp[:, 0, 2:4, :].rearrange("b w d -> b (w d)"), bank[0][0:B, :]))
            raw4 = mtmp[:, 0]
            link(v.tensor_copy(modrow[:, 1, :], raw4[:, 1, :]))
            link(v.tensor_scalar(modrow[:, 2, :], raw4[:, 2, :], 1.0, None, ALU.add))
            link(v.scalar_tensor_tensor(mtmp[:, 1, 0:4:3, :], raw4[:, 0:4:3, :], -1.0, raw4[:, 0:4:3, :], ALU.mult, ALU.max))
            link(v.tensor_scalar(mtmp[:, 2, 0:4:3, :], raw4[:, 0:4:3, :], 0.0, 2.0, ALU.is_ge, ALU.mult))
            link(v.tensor_scalar(mtmp[:, 2, 0:4:3, :], mtmp[:, 2, 0:4:3, :], -1.0, None, ALU.add))
            v.scalar_tensor_tensor(modrow[:, 0:4:3, :], mtmp[:, 1, 0:4:3, :], 0.25, mtmp[:, 2, 0:4:3, :], ALU.max, ALU.mult
                                   ).then_inc(s["modrow_ok"], 1)
            for i in (1, 3):
                v.wait_ge(s["qT_ps"], i + 1)
                v.tensor_scalar(qT[:, i // 2, (i % 2) * 512:(i % 2) * 512 + 512], bank[i][:], 0.25, 0.0, ALU.mult, ALU.max
                                ).then_inc(s["qT_v"], 1)
            for t in range(T):
                v.wait_ge(s["kvu_ps"], t + 1)
                bk = bank[4 + 2 * (t % 2)]
                v.tensor_scalar(kvu[:, t, 0, :], bk[:, 0:D], 0.25, 0.0, ALU.mult, ALU.max).then_inc(s["kvu_v"], 1)
                v.tensor_copy(kvu[:, t, 1, :], bk[:, D:2 * D]).then_inc(s["kvu_v"], 1)
            for b in range(B):
                v.wait_ge(s["kv_ps"], b + 1)
                v.tensor_tensor(kvm[:, b], bank[b][:, 0:KD * P].rearrange("p (k t) -> p k t", k=KD),
                                blockmask[:].unsqueeze(1).broadcast_to([P, KD, P]), ALU.mult).then_inc(s["kvm_ok"], 1)
            v.wait_ge(s["kvu_a"], T)
            for b in range(B):
                v.wait_ge(s["sq_ok"], b + 1)
                v.tensor_tensor(ou[:, TB * b:TB * b + TB, :], bank[4 + b][:].rearrange("p (t d) -> p t d", t=TB),
                                kvu[:, TB * b:TB * b + TB, 2, :], ALU.mult).then_inc(s["ou_ok"], 1)
                v.tensor_reduce(hn[:, TB * b:TB * b + TB, :],
                                sq[:, b % 2, :].rearrange("p (t h i) -> p t h i", t=TB, i=HD), AX.X, ALU.add
                                ).then_inc(s["hn_sum"], 1)
            v.wait_ge(s["hn_sqrt"], 1)
            link(v.tensor_scalar(hr[:], hn[:], 1e-12, None, ALU.max))
            link(v.reciprocal(hr[:], hr[:]))
            for b in range(B):
                o4 = ou[:, TB * b:TB * b + TB, :].rearrange("p t (h i) -> p (t h) i", i=HD)
                v.tensor_tensor(o4, o4, hr[:, TB * b:TB * b + TB, :].rearrange("p t h -> p (t h)").unsqueeze(2)
                                .broadcast_to([P, TB * NH, HD]), ALU.mult).then_inc(s["a_ok"], 1)
            for b in range(1, B, 2):
                v.wait_ge(s["aT_ps"], b + 1)
                v.tensor_copy(aT[:, :, b * L:(b + 1) * L], bank[4 + b][:].rearrange("p (k t) -> p k t", k=KD)
                              ).then_inc(s["aT_v"], 1)
            v.wait_ge(s["modB_ok"], 2 * B)
            for b in range(B):
                v.wait_ge(s["wo_ps"], b + 1)
                t2 = xn[:, TB * b:TB * b + TB, :]
                link(v.tensor_tensor(t2, bank[b][:].rearrange("p (t d) -> p t d", t=TB),
                                     modB[:, b, 0, :].unsqueeze(1).broadcast_to([P, TB, D]), ALU.mult))
                x2 = x_sb[:, TB * b:TB * b + TB, :]
                link(v.tensor_tensor(x2, x2, t2, ALU.add))
            norm_stats(x_sb, "mv2_ok")
            v.wait_ge(s["std2_ok"], 1)
            link(v.reciprocal(rstd[:], rstd[:]))
            for t in range(T):
                b = t // TB
                link(v.tensor_scalar(xn[:, t, :], x_sb[:, t, :], mv[:, t, 0:1], rstd[:, t:t + 1], ALU.subtract, ALU.mult))
                link(v.tensor_tensor(xn[:, t, :], xn[:, t, :], modB[:, b, 2, :], ALU.mult))
                v.tensor_tensor(xn[:, t, :], xn[:, t, :], modB[:, b, 1, :], ALU.add).then_inc(s["h2_ok"], 1)
            for b in range(B):
                v.wait_ge(s["h2hi"], b + 1)
                pk = bank[4 + b][:].rearrange("p (k t) -> p k t", k=KD)
                v.tensor_copy(hT[:, :, b * L:(b + 1) * L], pk).then_inc(s["lgT_ok"], 1)
                v.tensor_tensor(hTlo[:, :, b * L:(b + 1) * L], pk, hThi[:, :, b * L:(b + 1) * L].bitcast(f32), ALU.subtract
                                ).then_inc(s["h2lo"], 1)
            v.wait_ge(s["lg_ps"], 1)
            lps = bank[0][:, 0:T * E].rearrange("p (t e) -> p t e", e=E)

            def bc(ap):
                return ap.unsqueeze(2).broadcast_to([P, T, E])
            link(v.tensor_reduce(sm[:, 0], lps, AX.X, ALU.max))
            v.tensor_tensor(lg[:, 0], lps, bc(sm[:, 0]), ALU.subtract).then_inc(s["ex_in"], 1)
            v.wait_ge(s["ex_ok"], 1)
            link(v.tensor_reduce(sm[:, 1], lg[:, 1], AX.X, ALU.add))
            link(v.reciprocal(sm[:, 1], sm[:, 1]))
            link(v.tensor_tensor(lg[:, 1], lg[:, 1], bc(sm[:, 1]), ALU.mult))
            cur = lg[:, 1]
            for r in range(2):
                link(v.tensor_reduce(sm[:, 2 + r], cur, AX.X, ALU.max))
                link(v.tensor_tensor(lg[:, 2], cur, bc(sm[:, 2 + r]), ALU.is_equal))
                link(v.tensor_tensor(lg[:, 2], lg[:, 2], prio[:], ALU.mult))
                link(v.tensor_reduce(sm[:, 4], lg[:, 2], AX.X, ALU.max))
                link(v.tensor_tensor(lg[:, 3 + r], lg[:, 2], bc(sm[:, 4]), ALU.is_equal))
                if r == 0:
                    link(v.scalar_tensor_tensor(lg[:, 5], lg[:, 3], -2.0, cur, ALU.mult, ALU.add))
                    cur = lg[:, 5]
            link(v.tensor_tensor(sm[:, 5], sm[:, 2], sm[:, 3], ALU.add))
            link(v.tensor_scalar(sm[:, 5], sm[:, 5], 1e-20, None, ALU.add))
            link(v.reciprocal(sm[:, 5], sm[:, 5]))
            for r in range(2):
                link(v.tensor_tensor(sm[:, 6 + r], sm[:, 2 + r], sm[:, 5], ALU.mult))
                link(v.tensor_tensor(lg[:, 3 + r], lg[:, 3 + r], bc(sm[:, 6 + r]), ALU.mult))
            link(v.tensor_tensor(dw[:], lg[:, 3], lg[:, 4], ALU.add))

            def out_add(st):
                n, t = st // T, st % T
                v.wait_ge(s["y_ps"], st + 1)
                Y = bank[6 + st % 2][:, 0:D]
                if n == 0:
                    v.tensor_copy(y[:, t, :], Y).then_inc(s["y_ok"], 1)
                else:
                    v.wait_ge(s["y_ok"], st - T + 1)
                    v.scalar_tensor_tensor(y[:, t, :], Y, dw[:, t, n - 1:n], y[:, t, :], ALU.mult, ALU.add
                                           ).then_inc(s["y_ok"], 1)

            for st in range(NX * T):
                for q in range(2):
                    v.wait_ge(s["silu_ok"], 2 * st + q + 1)
                    v.tensor_tensor(actv[:, st % 2, q * FH:(q + 1) * FH], bank[2 * q][:, 0:FH], sil[:, q, :], ALU.mult
                                    ).then_inc(s["mul_ok"], 1)
                v.wait_ge(s["thi"], 2 * st + 1)
                v.tensor_tensor(aTlo[:, 0:4, :].rearrange("p c t -> p (c t)"), bank[4][:],
                                aThi[:, 0:4, :].rearrange("p c t -> p (c t)").bitcast(f32), ALU.subtract).then_inc(s["tlo"], 1)
                v.wait_ge(s["thi"], 2 * st + 2)
                v.tensor_tensor(aTlo[0:96, 4:6, :].rearrange("p c t -> p (c t)"), bank[5][0:96, 0:256],
                                aThi[0:96, 4:6, :].rearrange("p c t -> p (c t)").bitcast(f32), ALU.subtract
                                ).then_inc(s["tlo"], 1)
                out_add(st)
            for t in range(T):
                v.wait_ge(s["y_ok"], NX * T)
                link(v.tensor_tensor(y[:, t, :], y[:, t, :], modB[:, t // TB, 3, :], ALU.mult))
                v.tensor_tensor(y[:, t, :], y[:, t, :], x_sb[:, t, :], ALU.add).then_inc(s["y_ok"], 1)

        @block.tensor
        def _(pe):
            mm = pe.matmul
            pe.wait_ge(s["const"], 5)
            pe.wait_ge(s["silc"], 1)
            for k in range(KD):
                last = pe.transpose(bank[0][:, k * B:(k + 1) * B], sc_sb[:, k * P:(k + 1) * P], ident[0:B, 0:B])
            last.then_inc(s["cT"], 1)
            pe.wait_ge(s["d_gw"], 16)
            for k in range(KD):
                last = pe.transpose(bank[1][:, k * E:(k + 1) * E], gw_sb[:, k * P:(k + 1) * P], ident[0:E, 0:E])
            last.then_inc(s["gwT_ps"], 1)
            pe.wait_ge(s["scT_ok"], 1)
            pe.wait_ge(s["d_wmod"], 16)
            for m in range(4):
                for k in range(KD):
                    last = mm(bank[2][:, m * B:(m + 1) * B], wmod_sb[:, k, m * P:(m + 1) * P], scT[:, k, :],
                              start=(k == 0), stop=(k == KD - 1))
            last.then_inc(s["modT_ps"], 1)
            for i in range(2):
                for k in range(KD):
                    last = mm((bank[3], bank[0])[i][0:B, :], scT[:, k, :], wmod_sb[:, k, (i + 1) * 512:(i + 2) * 512],
                              start=(k == 0), stop=(k == KD - 1))
                last.then_inc(s["modrow_ps"], 1)
            for b in range(B):
                pe.wait_ge(s["xn_ok"], TB * (b + 1))
                for k in range(KD):
                    for t in range(TB):
                        last = pe.transpose(bank[4 + b][:, k * L + t * P:k * L + (t + 1) * P],
                                            xn[:, TB * b + t, k * P:(k + 1) * P], ident[:])
                last.then_inc(s["xT_ps"], 1)
            pe.wait_ge(s["d_wqkvu"], 64)
            pe.wait_ge(s["hT_a"], B)
            pe.wait_ge(s["hT_v"], B)
            pe.wait_ge(s["gwT_ok"], 1)
            pe.wait_ge(s["modrow_ok"], 1)
            for i in range(4):
                j, h = i // 2, i % 2
                for k in range(KD):
                    last = mm(bank[i][:], wqkvu[:, k, 0, j * P:(j + 1) * P], hT[:, k, h * 512:(h + 1) * 512],
                              start=(k == 0), stop=(k == KD - 1))
                last.then_inc(s["qT_ps"], 1)
            for t in range(T):
                if t >= 2:
                    pe.wait_ge(s["kvu_v"], 2 * (t - 1))
                    pe.wait_ge(s["kvu_a"], t - 1)
                for w, bk, n in ((1, 4, 2), (3, 5, 1)):
                    for k in range(KD):
                        last = mm(bank[bk + 2 * (t % 2)][:, 0:n * D], hT[:, k, t * P:(t + 1) * P],
                                  wqkvu[:, k, w:w + n, :].rearrange("p w d -> p (w d)"), start=(k == 0), stop=(k == KD - 1))
                last.then_inc(s["kvu_ps"], 1)
            pe.wait_ge(s["qT_a"], 2)
            pe.wait_ge(s["qT_v"], 2)
            for b in range(B):
                pe.wait_ge(s["kvu_v"], 2 * TB * (b + 1))
                for k in range(KD):
                    for t in range(TB):
                        last = mm(bank[b][:, k * P:(k + 1) * P], kvu[:, TB * b + t, 0, k * P:(k + 1) * P],
                                  kvu[:, TB * b + t, 1, k * P:(k + 1) * P], start=(t == 0), stop=(t == TB - 1))
                last.then_inc(s["kv_ps"], 1)
            pe.wait_ge(s["kvu_a"], T)
            for b in range(B):
                pe.wait_ge(s["kvm_ok"], b + 1)
                for t in range(TB):
                    for k in range(KD):
                        last = mm(bank[4 + b][:, t * D + k * P:t * D + (k + 1) * P], qT[:, k, (TB * b + t) * P:(TB * b + t + 1) * P],
                                  kvm[:, b, k, :], start=True, stop=True)
                last.then_inc(s["o_ps"], 1)
            pe.wait_ge(s["kvm_ok"], B)
            for i in range(2 * B):
                b, h = i // 2, i % 2
                if i >= 4:
                    pe.wait_ge(s["modB_ok"], i - 3)
                mm(bank[i % 4][:], sel[:, b, :], modrow[:, 2 * h:2 * h + 2, :].rearrange("b w d -> b (w d)"),
                   start=True, stop=True).then_inc(s["modB_ps"], 1)
            for b in range(B):
                pe.wait_ge(s["a_ok"], b + 1)
                for k in range(KD):
                    for t in range(TB):
                        last = pe.transpose(bank[4 + b][:, k * L + t * P:k * L + (t + 1) * P],
                                            ou[:, TB * b + t, k * P:(k + 1) * P], ident[:])
                last.then_inc(s["aT_ps"], 1)
            pe.wait_ge(s["d_wo"], 16)
            pe.wait_ge(s["modB_ok"], 2 * B)
            for b in range(B):
                pe.wait_ge(s["aT_v" if b % 2 else "aT_a"], b // 2 + 1)
                for t in range(TB):
                    for k in range(KD):
                        last = mm(bank[b][:, t * D:(t + 1) * D], aT[:, k, (TB * b + t) * P:(TB * b + t + 1) * P], wo_sb[:, k, :],
                                  start=(k == 0), stop=(k == KD - 1))
                last.then_inc(s["wo_ps"], 1)
            for b in range(B):
                pe.wait_ge(s["h2_ok"], TB * (b + 1))
                for k in range(KD):
                    for t in range(TB):
                        last = pe.transpose(bank[4 + b][:, k * L + t * P:k * L + (t + 1) * P],
                                            xn[:, TB * b + t, k * P:(k + 1) * P], ident[:])
                last.then_inc(s["h2T_ps"], 1)
            pe.wait_ge(s["lgT_ok"], B)
            for t in range(T):
                for k in range(KD):
                    last = mm(bank[0][:, t * E:(t + 1) * E], hT[:, k, t * P:(t + 1) * P], gwT[:, k, :],
                              start=(k == 0), stop=(k == KD - 1))
            last.then_inc(s["lg_ps"], 1)
            pe.wait_ge(s["h2lo"], B)
            pe.wait_ge(s["ex_in"], 1)

            def gate_up(st, q):
                n, t = st // T, st % T
                if st >= 1:
                    pe.wait_ge(s["mul_ok"], 2 * (st - 1) + q + 1)
                for k in range(KD):
                    for x_, ws in ((hThi, (hi_gu, lo_gu)), (hTlo, (hi_gu,))):
                        for w in (GATE, UP):
                            for wi, W in enumerate(ws):
                                last = mm(bank[2 * q + w][:, 0:FH], x_[:, k, t * P:(t + 1) * P],
                                          W[:, n % 2, k, w, q * FH:(q + 1) * FH],
                                          start=(k == 0 and x_ is hThi and wi == 0), stop=(k == KD - 1 and x_ is hTlo),
                                          skip_group_check=True)
                last.then_inc(s["gu_ps"], 1)

            def turn(st):
                pe.wait_ge(s["mul_ok"], 2 * st + 2)
                if st >= 1:
                    pe.wait_ge(s["tlo"], 2 * st)
                for ch in range(FC):
                    last = pe.transpose(bank[4 + ch // 4][0:FR[ch], (ch % 4) * P:(ch % 4 + 1) * P],
                                        actv[:, st % 2, FO[ch]:FO[ch] + FR[ch]], ident[:])
                last.then_inc(s["t_ps"], 1)

            def down(st):
                n = st // T
                pe.wait_ge(s["tlo"], 2 * st + 2)
                if st >= 2:
                    pe.wait_ge(s["y_ok"], st - 1)
                for ch in range(FC):
                    r = FR[ch]
                    for i, (a_, W) in enumerate(((aThi, hi_d), (aThi, lo_d), (aTlo, hi_d))):
                        last = mm(bank[6 + st % 2][:, 0:D], a_[0:r, ch, :], W[0:r, n % 2, ch, :],
                                  start=(ch == 0 and i == 0), stop=(ch == FC - 1 and i == 2))
                last.then_inc(s["y_ps"], 1)

            for st in range(NX * T):
                pe.wait_ge(s["split"], st // T + 1)
                gate_up(st, 0)
                if st:
                    turn(st - 1)
                gate_up(st, 1)
                if st:
                    down(st - 1)
            turn(NX * T - 1)
            down(NX * T - 1)


_INS = ['L0_attn_x', 'L0_attn_Wq', 'L0_attn_Wk', 'L0_attn_Wv', 'L0_attn_Wu', 'L0_attn_Wo', 'L0_ffn_gate_w',
        'L0_ffn_w_gate', 'L0_ffn_w_up', 'L0_ffn_w_down', 'L0_ffn_sw_gate', 'L0_ffn_sw_up', 'L0_ffn_sw_down',
        'L0_c', 'L0_wmod']


def kernel(**inputs):
    import numpy as _np
    import concourse.bacc as _bacc
    from concourse import mybir as _mybir
    from concourse.bass_utils import run_bass_kernel_spmd as _run

    nc = _bacc.Bacc("TRN2", target_bir_lowering=False, num_devices=1)
    arrays, args = {}, []
    for name in _INS:
        a = _np.ascontiguousarray(inputs[name])
        arrays[f"in_{name}_dram"] = a
        args.append(nc.dram_tensor(f"in_{name}_dram", a.shape, _mybir.dt.from_np(a.dtype), kind="ExternalInput").ap())
    out = nc.dram_tensor("out_0_dram", inputs['L0_attn_x'].shape, _mybir.dt.float32, kind="ExternalOutput").ap()
    adaln_block(nc, *args, out)
    r = _run(nc, [arrays], core_ids=[0])
    return r.results[0]["out_0_dram"]
```

```python
import concourse.bass as bass
from concourse import mybir
from contextlib import ExitStack


def adaln_block(nc, x, wq, wk, wv, wu, wo, gate_w, w_gate, w_up, w_down, sw_gate, sw_up, sw_down, c, wmod, out):
    f32 = mybir.dt.float32
    f32r = mybir.dt.float32r
    ALU = mybir.AluOpType
    ACT = mybir.ActivationFunctionType
    AX = mybir.AxisListType

    P = 128
    B, L, D = x.shape
    T = B * L // P
    TB = L // P
    KD = D // P
    HD = 16
    NH = D // HD
    E, _, F = w_gate.shape
    K = 2
    NR = (K * T * P + E * (P - 1)) // P
    SA, SB = 4, 4
    NX = E + 2
    NS = SA + NR + SB
    FA = 512
    FB = F - FA
    GU = KD * 2 * F
    FC = 6
    FR = [128, 128, 128, 128, 96, 96]
    FO = [0, 128, 256, 384, 512, 608]
    W1 = GU + FC * D
    EPS = 1e-5

    ctx = ExitStack()
    with ctx:
        def sb(name, shape, dt=f32):
            return ctx.enter_context(nc.sbuf_tensor(name, shape, dt))

        def sem(name):
            return ctx.enter_context(nc.semaphore(name))

        ident = sb("ident", [P, P])
        blockmask = sb("blockmask", [P, P])
        sel = sb("sel", [B, B, P])
        eps = sb("eps", [P, 1])
        triu = sb("triu", [P, P])
        ones = sb("ones", [P, P])
        zero = sb("zero", [P, D])
        keep = sb("keep", [P, E, T])
        steps128 = sb("steps128", [P, E, T])
        stepno = sb("stepno", [1, NR, E - 1])
        sign = sb("sign", [1, NR, E - 1])
        cnt = sb("cnt", [P, 4, E, T])
        pe_ = sb("per_expert", [P, 4, E])
        where = sb("where", [P, 2, T, E])
        posf = sb("posf", [P, K, T])
        pos = sb("pos", [P, K, T], mybir.dt.int32)
        ind = sb("ind", [1, 3, NR, E - 1])
        tabf = sb("tabf", [1, 3, NR])
        tab = sb("tab", [1, 3, NR], mybir.dt.int32)
        wtok = sb("wtok", [P, K, T])
        prio = sb("prio", [P, T, E])
        scT = sb("scT", [P, KD, B])
        modT = sb("modT", [P, 4, B])
        modrow = sb("modrow", [B, 4, D])
        gbB = sb("gbB", [P, B, D])
        gwT = sb("gwT", [P, KD, E])
        wo_sb = sb("wo_sb", [P, KD, D])
        x_sb = sb("x_sb", [P, T, D])
        xn = sb("xn", [P, T, D])
        hT = sb("hT", [P, KD, T * P])
        kvm = sb("kvm", [P, B, KD, P])
        ou = sb("ou", [P, T, D])
        stats = sb("stats", [P, T, 6])
        mv = sb("mv", [P, T, 2])
        rstd = sb("rstd", [P, T])
        hn = sb("hn", [P, T, NH])
        hr = sb("hr", [P, T, NH])
        lg = sb("lg", [P, 8, T, E])
        sm = sb("sm", [P, 8, T])
        raw = sb("raw", [P, 2, W1])
        whi = sb("whi", [P, 2 * W1], f32r)
        wlo = sb("wlo", [P, 2 * W1], f32r)
        aT = hT
        y = ou
        got = [xn, hT[:].rearrange("p k (t d) -> p (k t) d", d=D)]
        def front(name, shape):
            return attn.enter_context(nc.sbuf_tensor(name, shape, f32))
        attn = ExitStack()
        modB = front("modB", [P, B, 3, D])
        kvu = front("kvu", [P, T, 3, D])
        qT = front("qT", [P, KD, T * P])
        mtmp = kvu[0:B, 0:4].rearrange("b t w d -> b (t w d)").rearrange("b (r w d) -> b r w d", r=3, w=4)
        c_sb, sc_sb, gw_sb = kvu[0:B, 4, 0], kvu[0:B, 4, 1], kvu[0:E, 4, 2]
        sq = hT[:, 0].rearrange("p (i d) -> p i d", i=2)
        wqkvu = ou[:].rearrange("p (k w) d -> p k w d", k=KD)
        wmod_sb = raw[:, 1, 0:KD * 6 * D].rearrange("p (k n) -> p k n", k=KD)
        attn.close()
        sil = sb("sil", [P, F])
        actv = sb("actv", [P, 2, F])
        xg = sb("xg", [P, 2, D])
        xThi = sb("xThi", [P, 2, KD, P], f32r)
        xTlo = sb("xTlo", [P, 2, KD, P], f32r)
        yst = sb("yst", [P, 2, D])
        aThi = sb("aThi", [P, FC, P], f32r)
        aTlo = sb("aTlo", [P, FC, P], f32r)
        hThi = sb("hThi", [P, KD, T * P], f32r)
        hTlo = sb("hTlo", [P, KD, T * P], f32r)

        slots = nc.dram_tensor("slots", [NR * P, D], f32, kind="Internal").ap()
        results = nc.dram_tensor("results", [NR * P, D], f32, kind="Internal").ap()
        bank = [ctx.enter_context(nc.psum_tensor(f"bank{i}", [P, 512], f32)) for i in range(8)]

        names = ("d_c d_gw d_wmod d_wqkvu d_wo d_out const silc cT scT_ok gwT_ps gwT_ok modT_ps modT_ok modrow_ps "
                 "modrow_ok mv_ok std_ok xn_ok xT_ps hT_a hT_v qT_ps qT_a qT_v kvu_ps kvu_v kvu_a kv_ps kvm_ok o_ps sq_ok "
                 "ou_ok hn_sum hn_sqrt a_ok modB_ps modB_ok aT_ps aT_a aT_v wo_ps x2_ok mv2_ok std2_ok xn2_ok h2_ok "
                 "h2T_ps h2hi h2lo lgT_ok lg_ps ex_in ex_ok dw_ok dch ach pch split gu_ps silu_ok mul_ok t_ps thi tlo "
                 "y_ps y_ok raw_used zero_ok d_zero place_free d_scat d_got mask_ok rank_ps pos_ok tab_ok x_ps xhi xlo ycopy").split()
        s = {n: sem(n) for n in names}
        d_x = [sem(f"d_x{b}") for b in range(B)]
        d_raw = [sem(f"d_raw{i}") for i in range(2)]
        d_xg = [sem(f"d_xg{i}") for i in range(2)]
        d_yst = [sem(f"d_yst{i}") for i in range(2)]

        raw_gu = raw[:, :, 0:GU].rearrange("p s (k w f) -> p s k w f", k=KD, w=2)
        raw_d = raw[:, :, GU:W1].rearrange("p s (c d) -> p s c d", c=FC)

        def gu_at(w, off, k, which, c0, n):
            return w[:, bass.ds(off + ((k * 2 + which) * F + c0), n)]

        def down_at(w, off, ch):
            return w[0:FR[ch], bass.ds(off + (GU + ch * D), D)]
        GATE, UP = 0, 1

        block = ctx.enter_context(nc.Block())

        @block.sync
        def _(sp):
            sp.dma_start(c_sb[:], c).then_inc(s["d_c"], 16)
            for b in range(B):
                sp.dma_start(x_sb[:, TB * b:TB * b + TB, :], x[b].rearrange("(t p) d -> p t d", p=P)).then_inc(d_x[b], 16)
            sp.dma_start(wmod_sb[:], wmod.rearrange("(k p) n -> p k n", p=P)).then_inc(s["d_wmod"], 16)
            sp.dma_start(gw_sb[:], gate_w).then_inc(s["d_gw"], 16)
            for i, w in enumerate((wq, wk, wv, wu)):
                sp.dma_start(wqkvu[:, :, i, :], w.rearrange("(k p) n -> p k n", p=P)).then_inc(s["d_wqkvu"], 16)
            sp.dma_start(wo_sb[:], wo.rearrange("(k p) n -> p k n", p=P)).then_inc(s["d_wo"], 16)
            for n in range(NX):
                g, u, d = (sw_gate[0], sw_up[0], sw_down[0]) if n in (0, NX - 1) else (w_gate[n - 1], w_up[n - 1], w_down[n - 1])
                sl = n % 2
                if n >= 2:
                    sp.wait_ge(s["raw_used"], n - 1)
                if n == 0:
                    sp.wait_ge(s["zero_ok"], 3)
                if n == 1:
                    sp.wait_ge(s["modrow_ps"], 2)
                sp.dma_start(raw_gu[:, sl, :, GATE, :], g.rearrange("(k p) f -> p k f", p=P)).then_inc(d_raw[n % 2], 16)
                sp.dma_start(raw_gu[:, sl, :, UP, :], u.rearrange("(k p) f -> p k f", p=P)).then_inc(d_raw[n % 2], 16)
                sp.dma_start(raw_d[:, sl, 0:4, :], d[0:512].rearrange("(c p) d -> p c d", p=P)).then_inc(d_raw[n % 2], 16)
                sp.dma_start(raw_d[0:96, sl, 4:6, :], d[512:704].rearrange("(c p) d -> p c d", p=96)).then_inc(d_raw[n % 2], 16)
                if n == 1:
                    sp.dma_start(slots.rearrange("(i p) d -> p i d", p=P), zero[:].unsqueeze(1).broadcast_to([P, NR, D])
                                 ).then_inc(s["d_zero"], 16)
            ov = out.rearrange("b (t p) d -> p (b t) d", p=P)
            for t in range(T):
                sp.wait_ge(s["y_ok"], T + t + 1)
                sp.dma_start(ov[:, t, :], y[:, t, :]).then_inc(s["d_out"], 16)
            sp.wait_ge(s["d_out"], 16 * T)

        @block.gpsimd
        def _(pool):
            chain = [0]

            def link(ins):
                chain[0] += 1
                ins.then_inc(s["pch"], 1)
                pool.wait_ge(s["pch"], chain[0])
            link(pool.memset(ident[:], 1.0))
            pool.affine_select(out=ident[:], in_=ident[:], compare_op=ALU.is_equal, fill=0.0, base=0,
                               pattern=[[-1, P]], channel_multiplier=1).then_inc(s["const"], 1)
            pool.memset(eps[:], EPS).then_inc(s["const"], 1)
            link(pool.memset(sel[:], 1.0))
            pool.affine_select(out=sel[:], in_=sel[:], compare_op=ALU.is_equal, fill=0.0, base=0,
                               pattern=[[-1, B], [0, P]], channel_multiplier=1).then_inc(s["const"], 1)
            link(pool.memset(blockmask[:], 1.0))
            bm = blockmask[:].rearrange("p (j i) -> p j i", i=HD)
            link(pool.affine_select(out=bm, in_=bm, compare_op=ALU.is_ge, fill=0.0, base=0,
                                    pattern=[[-HD, P // HD], [0, HD]], channel_multiplier=1))
            pool.affine_select(out=bm, in_=bm, compare_op=ALU.is_ge, fill=0.0, base=HD - 1,
                               pattern=[[HD, P // HD], [0, HD]], channel_multiplier=-1).then_inc(s["const"], 1)
            pool.iota(prio[:], pattern=[[0, T], [-1, E]], base=E, channel_multiplier=0,
                      allow_small_or_imprecise_dtypes=True).then_inc(s["const"], 1)
            pool.memset(ones[:], 1.0).then_inc(s["const"], 1)
            link(pool.memset(triu[:], 1.0))
            pool.affine_select(out=triu[:], in_=triu[:], compare_op=ALU.is_gt, fill=0.0, base=0,
                               pattern=[[1, P]], channel_multiplier=-1).then_inc(s["const"], 1)
            link(pool.memset(keep[:], 1.0))
            pool.memset(keep[:, :, 0], 0.0).then_inc(s["const"], 1)
            pool.iota(steps128[:], pattern=[[0, E], [P, T]], base=0, channel_multiplier=0,
                      allow_small_or_imprecise_dtypes=True).then_inc(s["const"], 1)
            pool.iota(stepno[:], pattern=[[1, NR], [0, E - 1]], base=0, channel_multiplier=0,
                      allow_small_or_imprecise_dtypes=True).then_inc(s["const"], 1)
            link(pool.memset(sign[:], 1.0))
            pool.memset(sign[:, :, 1:E - 1:2], -1.0).then_inc(s["const"], 1)

            def split(n):
                w = slice((n % 2) * W1, (n % 2 + 1) * W1)
                pool.wait_ge(d_raw[n % 2], 64 * (n // 2 + 1))
                link(pool.tensor_scalar(whi[:, w], raw[:, n % 2, :], 1.0, 0.0, ALU.mult, ALU.add))
                pool.tensor_tensor(wlo[:, w], raw[:, n % 2, :], whi[:, w].bitcast(f32), ALU.subtract).then_inc(s["split"], 1)
                pool.wait_ge(s["split"], n + 1)
                pool.sem_inc(s["raw_used"], 1)

            split(0)
            split(1)
            pool.wait_ge(s["d_zero"], 16)
            pool.wait_ge(s["h2_ok"], T)
            pool.wait_ge(s["pos_ok"], 1)
            for t in range(T):
                for k in range(K):
                    pool.indirect_dma_start(out=slots, out_offset=bass.IndirectOffsetOnAxis(ap=pos[:, k, t:t + 1], axis=0),
                                            in_=xn[:, t, :], in_offset=None).then_inc(s["d_scat"], 16)
            pool.wait_ge(s["y_ps"], SA)
            split(2)
            pool.wait_ge(s["tab_ok"], 1)
            for n in range(3, NX):
                pool.wait_ge(s["y_ps"], pool.value_load(tab[0:1, 2, n - 3:n - 2], min_val=SA, max_val=SA + NR))
                pool.sem_inc(s["place_free"], 1)
                pool.wait_ge(s["place_free"], n - 2)
                split(n)
            for i in range(2):
                pool.wait_ge(d_yst[i], 16 * ((NR + 1 - i) // 2))
            pool.wait_ge(s["d_scat"], 16 * K * T)
            pool.wait_ge(s["lg_ps"], 1)
            for t in range(T):
                for k in range(K):
                    pool.indirect_dma_start(out=got[k][:, t, :], out_offset=None, in_=results,
                                            in_offset=bass.IndirectOffsetOnAxis(ap=pos[:, k, t:t + 1], axis=0)
                                            ).then_inc(s["d_got"], 16)

        @block.scalar
        def _(act_e):
            a = act_e
            a.wait_ge(s["d_c"], 16)
            a.activation(sc_sb[:], c_sb[:], ACT.Silu).then_inc(s["silc"], 1)
            a.wait_ge(s["const"], 11)
            a.wait_ge(s["mv_ok"], T)
            a.activation(rstd[:], mv[:, :, 1], ACT.Sqrt, bias=eps[:]).then_inc(s["std_ok"], 1)
            a.wait_ge(s["modT_ok"], 2)
            for b in range(0, B, 2):
                a.wait_ge(s["xT_ps"], b + 1)
                for k in range(KD):
                    a.activation(hT[:, k, b * L:(b + 1) * L], bank[4 + b][:, k * L:(k + 1) * L], ACT.Identity,
                                 scale=modT[:, 2 + k, b:b + 1], bias=modT[:, k, b:b + 1]).then_inc(s["hT_a"], 1)
            for i in (0, 2):
                a.wait_ge(s["qT_ps"], i + 1)
                a.activation(qT[:, i // 2, (i % 2) * 512:(i % 2) * 512 + 512], bank[i][:], ACT.Relu, scale=0.25
                             ).then_inc(s["qT_a"], 1)
            for t in range(T):
                a.wait_ge(s["kvu_ps"], t + 1)
                a.activation(kvu[:, t, 2, :], bank[5 + 2 * (t % 2)][:, 0:D], ACT.Silu).then_inc(s["kvu_a"], 1)
            for b in range(B):
                a.wait_ge(s["o_ps"], b + 1)
                if b >= 2:
                    a.wait_ge(s["hn_sum"], b - 1)
                a.activation(sq[:, b % 2, :], bank[4 + b][:], ACT.Square).then_inc(s["sq_ok"], 1)
            for i in range(2 * B):
                a.wait_ge(s["modB_ps"], i + 1)
                b, h = i // 2, i % 2
                if h == 0:
                    a.activation(modB[:, b, 0:2, :].rearrange("p w d -> p (w d)"), bank[i % 4][:], ACT.Copy
                                 ).then_inc(s["modB_ok"], 1)
                else:
                    a.activation(modB[:, b, 2, :], bank[i % 4][:, 0:D], ACT.Copy)
                    a.activation(gbB[:, b, :], bank[i % 4][:, D:2 * D], ACT.Copy).then_inc(s["modB_ok"], 1)
            a.wait_ge(s["hn_sum"], B)
            a.activation(hn[:], hn[:], ACT.Sqrt, scale=1.0 / HD).then_inc(s["hn_sqrt"], 1)
            for b in range(0, B, 2):
                a.wait_ge(s["aT_ps"], b + 1)
                a.activation(aT[:, :, b * L:(b + 1) * L], bank[4 + b][:].rearrange("p (k t) -> p k t", k=KD), ACT.Copy
                             ).then_inc(s["aT_a"], 1)
            a.wait_ge(s["mv2_ok"], T)
            a.activation(rstd[:], mv[:, :, 1], ACT.Sqrt, bias=eps[:]).then_inc(s["std2_ok"], 1)
            for b in range(B):
                a.wait_ge(s["h2T_ps"], b + 1)
                a.activation(hThi[:, :, b * L:(b + 1) * L], bank[4 + b][:].rearrange("p (k t) -> p k t", k=KD), ACT.Copy
                             ).then_inc(s["h2hi"], 1)
            a.wait_ge(s["ex_in"], 1)
            a.activation(lg[:, 1], lg[:, 0], ACT.Exp).then_inc(s["ex_ok"], 1)

            def load_x(i, par):
                a.dma_start(xg[:, par, :], slots[bass.ds(i * P, P), :]).then_inc(d_xg[par], 16)

            def silu(st, part):
                a.wait_ge(s["gu_ps"], 2 * st + part + 1)
                if part == 0:
                    a.activation(sil[:, 0:FA], bank[1][:], ACT.Silu).then_inc(s["silu_ok"], 1)
                else:
                    a.activation(sil[:, FA:F], bank[2][:, FB:2 * FB], ACT.Silu).then_inc(s["silu_ok"], 1)

            def turned(st):
                a.wait_ge(s["t_ps"], st + 1)
                a.activation(aThi[:, 0:4, :], bank[4][:], ACT.Copy).then_inc(s["thi"], 1)
                a.activation(aThi[0:96, 4:6, :], bank[5][0:96, 0:256], ACT.Copy).then_inc(s["thi"], 1)

            def rows_in(i, par, more):
                a.wait_ge(s["x_ps"], i + 1)
                a.activation(xThi[:, par], bank[3][:, 0:KD * P].rearrange("p (k t) -> p k t", k=KD), ACT.Copy
                             ).then_inc(s["xhi"], 1)
                if more:
                    load_x(i + 2, par)

            def rows_out(i, par, reused):
                a.wait_ge(s["y_ps"], i + (SA + 1))
                if reused is not None:
                    a.wait_ge(d_yst[par], reused)
                a.activation(yst[:, par, :], bank[6 + (SA + par) % 2][:, 0:D], ACT.Copy).then_inc(s["ycopy"], 1)
                a.wait_ge(s["ycopy"], i + 1)
                a.dma_start(results[bass.ds(i * P, P), :], yst[:, par, :]).then_inc(d_yst[par], 16)

            def step(st, par, i, i_in, more, i_out, reused):
                silu(st, 0)
                if not isinstance(st, int) or st:
                    turned(st - 1)
                silu(st, 1)
                if i_in:
                    rows_in(i + 1, 1 - par, more)
                if i_out:
                    rows_out(i - 1, 1 - par, reused)

            for st in range(SA - 1):
                step(st, st % 2, 0, False, False, False, None)
            a.wait_ge(s["d_scat"], 16 * K * T)
            load_x(0, 0)
            load_x(1, 1)
            step(SA - 1, 1, -1, True, True, False, None)
            step(SA, 0, 0, True, True, False, None)
            step(SA + 1, 1, 1, True, True, True, None)
            step(SA + 2, 0, 2, True, True, True, None)
            pairs = (NR - 7) // 2
            with a.Fori(0, pairs) as j:
                step(2 * j + (SA + 3), 1, 2 * j + 3, True, True, True, 16 * j + 16)
                step(2 * j + (SA + 4), 0, 2 * j + 4, True, True, True, 16 * j + 16)
            for i in range(2 * pairs + 3, NR + 1):
                step(SA + i, i % 2, i, i + 1 < NR, i + 3 < NR, True, 16 * ((i - 1) // 2))
            for st in range(SA + NR + 1, NS):
                step(st, st % 2, 0, False, False, False, None)
            turned(NS - 1)
            for t in range(T):
                a.wait_ge(s["d_got"], 16 * K * T)
                a.activation(got[0][:, t, :], got[0][:, t, :], ACT.Copy, scale=wtok[:, 0, t:t + 1]).then_inc(s["ach"], 1)

        @block.vector
        def _(v):
            chain = [0]

            def link(ins):
                chain[0] += 1
                ins.then_inc(s["dch"], 1)
                v.wait_ge(s["dch"], chain[0])

            def norm_stats(src, ok):
                for t in range(T):
                    v.bn_stats(stats[:, t, :], src[:, t, :]).then_inc(s["dch"], 1)
                    chain[0] += 1
                v.wait_ge(s["dch"], chain[0])
                for t in range(T):
                    v.bn_aggr(mv[:, t, :], stats[:, t, :]).then_inc(s[ok], 1)

            for i in range(2):
                v.memset(raw[96:128, i, GU + 4 * D:W1], 0.0).then_inc(s["zero_ok"], 1)
            v.memset(zero[:], 0.0).then_inc(s["zero_ok"], 1)
            for b in range(B):
                v.wait_ge(d_x[b], 16)
            norm_stats(x_sb, "mv_ok")
            v.wait_ge(s["std_ok"], 1)
            link(v.reciprocal(rstd[:], rstd[:]))
            for t in range(T):
                v.tensor_scalar(xn[:, t, :], x_sb[:, t, :], mv[:, t, 0:1], rstd[:, t:t + 1], ALU.subtract, ALU.mult
                                ).then_inc(s["xn_ok"], 1)
            v.wait_ge(s["cT"], 1)
            v.tensor_copy(scT[:], bank[0][:, 0:KD * B].rearrange("p (k b) -> p k b", k=KD)).then_inc(s["scT_ok"], 1)
            v.wait_ge(s["gwT_ps"], 1)
            v.tensor_copy(gwT[:], bank[1][:, 0:KD * E].rearrange("p (k e) -> p k e", k=KD)).then_inc(s["gwT_ok"], 1)
            v.wait_ge(s["modT_ps"], 1)
            v.tensor_copy(modT[:, 0:2, :], bank[2][:, 0:2 * B].rearrange("p (k b) -> p k b", b=B)).then_inc(s["modT_ok"], 1)
            v.tensor_scalar(modT[:, 2:4, :], bank[2][:, 2 * B:4 * B].rearrange("p (k b) -> p k b", b=B), 1.0, None, ALU.add
                            ).then_inc(s["modT_ok"], 1)
            v.wait_ge(s["modT_ok"], 2)
            for b in range(1, B, 2):
                v.wait_ge(s["xT_ps"], b + 1)
                for k in range(KD):
                    v.tensor_scalar(hT[:, k, b * L:(b + 1) * L], bank[4 + b][:, k * L:(k + 1) * L],
                                    modT[:, 2 + k, b:b + 1], modT[:, k, b:b + 1], ALU.mult, ALU.add).then_inc(s["hT_v"], 1)
            v.wait_ge(s["modrow_ps"], 1)
            link(v.tensor_copy(mtmp[:, 0, 0:2, :].rearrange("b w d -> b (w d)"), bank[3][0:B, :]))
            v.wait_ge(s["modrow_ps"], 2)
            link(v.tensor_copy(mtmp[:, 0, 2:4, :].rearrange("b w d -> b (w d)"), bank[0][0:B, :]))
            raw4 = mtmp[:, 0]
            link(v.tensor_copy(modrow[:, 1, :], raw4[:, 1, :]))
            link(v.tensor_scalar(modrow[:, 2, :], raw4[:, 2, :], 1.0, None, ALU.add))
            link(v.scalar_tensor_tensor(mtmp[:, 1, 0:4:3, :], raw4[:, 0:4:3, :], -1.0, raw4[:, 0:4:3, :], ALU.mult, ALU.max))
            link(v.tensor_scalar(mtmp[:, 2, 0:4:3, :], raw4[:, 0:4:3, :], 0.0, 2.0, ALU.is_ge, ALU.mult))
            link(v.tensor_scalar(mtmp[:, 2, 0:4:3, :], mtmp[:, 2, 0:4:3, :], -1.0, None, ALU.add))
            v.scalar_tensor_tensor(modrow[:, 0:4:3, :], mtmp[:, 1, 0:4:3, :], 0.25, mtmp[:, 2, 0:4:3, :], ALU.max, ALU.mult
                                   ).then_inc(s["modrow_ok"], 1)
            for i in (1, 3):
                v.wait_ge(s["qT_ps"], i + 1)
                v.tensor_scalar(qT[:, i // 2, (i % 2) * 512:(i % 2) * 512 + 512], bank[i][:], 0.25, 0.0, ALU.mult, ALU.max
                                ).then_inc(s["qT_v"], 1)
            for t in range(T):
                v.wait_ge(s["kvu_ps"], t + 1)
                bk = bank[4 + 2 * (t % 2)]
                v.tensor_scalar(kvu[:, t, 0, :], bk[:, 0:D], 0.25, 0.0, ALU.mult, ALU.max).then_inc(s["kvu_v"], 1)
                v.tensor_copy(kvu[:, t, 1, :], bk[:, D:2 * D]).then_inc(s["kvu_v"], 1)
            for b in range(B):
                v.wait_ge(s["kv_ps"], b + 1)
                v.tensor_tensor(kvm[:, b], bank[b][:, 0:KD * P].rearrange("p (k t) -> p k t", k=KD),
                                blockmask[:].unsqueeze(1).broadcast_to([P, KD, P]), ALU.mult).then_inc(s["kvm_ok"], 1)
            v.wait_ge(s["kvu_a"], T)
            for b in range(B):
                v.wait_ge(s["sq_ok"], b + 1)
                v.tensor_tensor(ou[:, TB * b:TB * b + TB, :], bank[4 + b][:].rearrange("p (t d) -> p t d", t=TB),
                                kvu[:, TB * b:TB * b + TB, 2, :], ALU.mult).then_inc(s["ou_ok"], 1)
                v.tensor_reduce(hn[:, TB * b:TB * b + TB, :],
                                sq[:, b % 2, :].rearrange("p (t h i) -> p t h i", t=TB, i=HD), AX.X, ALU.add
                                ).then_inc(s["hn_sum"], 1)
            v.wait_ge(s["hn_sqrt"], 1)
            link(v.tensor_scalar(hr[:], hn[:], 1e-12, None, ALU.max))
            link(v.reciprocal(hr[:], hr[:]))
            for b in range(B):
                o4 = ou[:, TB * b:TB * b + TB, :].rearrange("p t (h i) -> p (t h) i", i=HD)
                v.tensor_tensor(o4, o4, hr[:, TB * b:TB * b + TB, :].rearrange("p t h -> p (t h)").unsqueeze(2)
                                .broadcast_to([P, TB * NH, HD]), ALU.mult).then_inc(s["a_ok"], 1)
            for b in range(1, B, 2):
                v.wait_ge(s["aT_ps"], b + 1)
                v.tensor_copy(aT[:, :, b * L:(b + 1) * L], bank[4 + b][:].rearrange("p (k t) -> p k t", k=KD)
                              ).then_inc(s["aT_v"], 1)
            v.wait_ge(s["modB_ok"], 2 * B)
            for b in range(B):
                v.wait_ge(s["wo_ps"], b + 1)
                t2 = xn[:, TB * b:TB * b + TB, :]
                link(v.tensor_tensor(t2, bank[b][:].rearrange("p (t d) -> p t d", t=TB),
                                     modB[:, b, 0, :].unsqueeze(1).broadcast_to([P, TB, D]), ALU.mult))
                x2 = x_sb[:, TB * b:TB * b + TB, :]
                link(v.tensor_tensor(x2, x2, t2, ALU.add))
            norm_stats(x_sb, "mv2_ok")
            v.wait_ge(s["std2_ok"], 1)
            link(v.reciprocal(rstd[:], rstd[:]))
            for t in range(T):
                b = t // TB
                link(v.tensor_scalar(xn[:, t, :], x_sb[:, t, :], mv[:, t, 0:1], rstd[:, t:t + 1], ALU.subtract, ALU.mult))
                link(v.tensor_tensor(xn[:, t, :], xn[:, t, :], modB[:, b, 2, :], ALU.mult))
                v.tensor_tensor(xn[:, t, :], xn[:, t, :], modB[:, b, 1, :], ALU.add).then_inc(s["h2_ok"], 1)
            for b in range(B):
                v.wait_ge(s["h2hi"], b + 1)
                pk = bank[4 + b][:].rearrange("p (k t) -> p k t", k=KD)
                v.tensor_copy(hT[:, :, b * L:(b + 1) * L], pk).then_inc(s["lgT_ok"], 1)
                v.tensor_tensor(hTlo[:, :, b * L:(b + 1) * L], pk, hThi[:, :, b * L:(b + 1) * L].bitcast(f32), ALU.subtract
                                ).then_inc(s["h2lo"], 1)
            v.wait_ge(s["lg_ps"], 1)
            lps = bank[0][:, 0:T * E].rearrange("p (t e) -> p t e", e=E)

            def bc(ap):
                return ap.unsqueeze(2).broadcast_to([P, T, E])
            link(v.tensor_reduce(sm[:, 0], lps, AX.X, ALU.max))
            v.tensor_tensor(lg[:, 0], lps, bc(sm[:, 0]), ALU.subtract).then_inc(s["ex_in"], 1)
            v.wait_ge(s["ex_ok"], 1)
            link(v.tensor_reduce(sm[:, 1], lg[:, 1], AX.X, ALU.add))
            link(v.reciprocal(sm[:, 1], sm[:, 1]))
            link(v.tensor_tensor(lg[:, 1], lg[:, 1], bc(sm[:, 1]), ALU.mult))
            cur = lg[:, 1]
            for r in range(2):
                link(v.tensor_reduce(sm[:, 2 + r], cur, AX.X, ALU.max))
                link(v.tensor_tensor(lg[:, 2], cur, bc(sm[:, 2 + r]), ALU.is_equal))
                link(v.tensor_tensor(lg[:, 2], lg[:, 2], prio[:], ALU.mult))
                link(v.tensor_reduce(sm[:, 4], lg[:, 2], AX.X, ALU.max))
                link(v.tensor_tensor(lg[:, 3 + r], lg[:, 2], bc(sm[:, 4]), ALU.is_equal))
                if r == 0:
                    link(v.scalar_tensor_tensor(lg[:, 5], lg[:, 3], -2.0, cur, ALU.mult, ALU.add))
                    cur = lg[:, 5]
            v.tensor_tensor(lg[:, 6], lg[:, 3], lg[:, 4], ALU.add).then_inc(s["mask_ok"], 1)
            v.wait_ge(s["rank_ps"], 1)
            tot = bank[0][:, 2 * T * E:3 * T * E].rearrange("p (t e) -> p e t", e=E)
            link(v.tensor_copy(cnt[:, 0], tot))
            link(v.tensor_tensor_scan(cnt[:, 1].rearrange("p e t -> p (e t)"), keep[:].rearrange("p e t -> p (e t)"),
                                      cnt[:, 0].rearrange("p e t -> p (e t)"), 0.0, ALU.mult, ALU.add))
            link(v.tensor_tensor(cnt[:, 2], cnt[:, 1, :, T - 1:T].broadcast_to([P, E, T]), steps128[:], ALU.is_gt))
            link(v.tensor_reduce(pe_[:, 0], cnt[:, 2], AX.X, ALU.add))
            link(v.tensor_tensor_scan(pe_[:, 1], ones[:, 0:E], pe_[:, 0], 0.0, ALU.mult, ALU.add))
            link(v.tensor_tensor(pe_[:, 2], pe_[:, 1], pe_[:, 0], ALU.subtract))
            link(v.tensor_tensor(cnt[:, 3], cnt[:, 1], cnt[:, 0], ALU.subtract))
            link(v.scalar_tensor_tensor(cnt[:, 3], pe_[:, 2].unsqueeze(2).broadcast_to([P, E, T]), float(P), cnt[:, 3],
                                        ALU.mult, ALU.add))
            link(v.tensor_tensor(where[:, 0], bank[0][:, T * E:2 * T * E].rearrange("p (t e) -> p t e", e=E),
                                 cnt[:, 3].rearrange("p e t -> p t e"), ALU.add))
            for k in range(K):
                link(v.tensor_tensor(where[:, 1], where[:, 0], lg[:, 3 + k], ALU.mult))
                link(v.tensor_reduce(posf[:, k], where[:, 1], AX.X, ALU.add))
            v.tensor_copy(pos[:], posf[:]).then_inc(s["pos_ok"], 1)
            link(v.tensor_tensor(ind[:, 0], pe_[0:1, 1, 0:E - 1].unsqueeze(1).broadcast_to([1, NR, E - 1]), stepno[:],
                                 ALU.is_le))
            link(v.tensor_reduce(tabf[:, 1], ind[:, 0], AX.X, ALU.add))
            link(v.tensor_tensor(ind[:, 1], ind[:, 0], sign[:], ALU.mult))
            link(v.tensor_reduce(tabf[:, 0], ind[:, 1], AX.X, ALU.add))
            link(v.tensor_scalar(tab[:, 0], tabf[:, 0], -float(W1), float(W1), ALU.mult, ALU.add))
            link(v.tensor_scalar(tab[:, 1], tabf[:, 1], 2.0, None, ALU.add))
            v.tensor_scalar(tab[:, 2, 0:E], pe_[0:1, 1], float(SA), None, ALU.add).then_inc(s["tab_ok"], 1)
            link(v.tensor_tensor(sm[:, 5], sm[:, 2], sm[:, 3], ALU.add))
            link(v.tensor_scalar(sm[:, 5], sm[:, 5], 1e-20, None, ALU.add))
            link(v.reciprocal(sm[:, 5], sm[:, 5]))
            for k in range(K):
                link(v.tensor_tensor(wtok[:, k], sm[:, 2 + k], sm[:, 5], ALU.mult))

            def product(st, part, par):
                v.wait_ge(s["silu_ok"], 2 * st + part + 1)
                if part == 0:
                    v.tensor_tensor(actv[:, par, 0:FA], bank[0][:], sil[:, 0:FA], ALU.mult).then_inc(s["mul_ok"], 1)
                else:
                    v.tensor_tensor(actv[:, par, FA:F], bank[2][:, 0:FB], sil[:, FA:F], ALU.mult).then_inc(s["mul_ok"], 1)

            def low_parts(st):
                v.wait_ge(s["thi"], 2 * st + 1)
                v.tensor_tensor(aTlo[:, 0:4, :].rearrange("p c t -> p (c t)"), bank[4][:],
                                aThi[:, 0:4, :].rearrange("p c t -> p (c t)").bitcast(f32), ALU.subtract).then_inc(s["tlo"], 1)
                v.wait_ge(s["thi"], 2 * st + 2)
                v.tensor_tensor(aTlo[0:96, 4:6, :].rearrange("p c t -> p (c t)"), bank[5][0:96, 0:256],
                                aThi[0:96, 4:6, :].rearrange("p c t -> p (c t)").bitcast(f32), ALU.subtract
                                ).then_inc(s["tlo"], 1)

            def shared_out(st):
                t = st if st < SA else st - NR
                v.wait_ge(s["y_ps"], st + 1)
                link(v.tensor_tensor(y[:, t, :], bank[6 + st % 2][:, 0:D], gbB[:, t // TB, :], ALU.mult))
                v.tensor_tensor(y[:, t, :], y[:, t, :], x_sb[:, t, :], ALU.add).then_inc(s["y_ok"], 1)

            def step(st, par, i, i_in, out_st):
                product(st, 0, par)
                if not isinstance(st, int) or st:
                    low_parts(st - 1)
                product(st, 1, par)
                if i_in:
                    xp = 1 - par
                    v.wait_ge(s["xhi"], i + 2)
                    v.tensor_tensor(xTlo[:, xp], bank[3][:, 0:KD * P].rearrange("p (k t) -> p k t", k=KD),
                                    xThi[:, xp].bitcast(f32), ALU.subtract).then_inc(s["xlo"], 1)
                if out_st is not None:
                    shared_out(out_st)

            for st in range(SA):
                step(st, st % 2, -1, st == SA - 1, st - 1 if st else None)
            step(SA, SA % 2, 0, True, SA - 1)
            with v.Fori(0, (NR - 3) // 2) as j:
                step(2 * j + (SA + 1), (SA + 1) % 2, 2 * j + 1, True, None)
                step(2 * j + (SA + 2), SA % 2, 2 * j + 2, True, None)
            step(SA + NR - 2, (SA + NR) % 2, NR - 2, True, None)
            step(SA + NR - 1, (SA + NR - 1) % 2, NR - 1, False, None)
            for st in range(SA + NR, NS):
                step(st, st % 2, 0, False, st - 1 if st > SA + NR else None)
            low_parts(NS - 1)
            shared_out(NS - 1)
            v.wait_ge(s["d_got"], 16 * K * T)
            for t in range(T):
                v.wait_ge(s["ach"], t + 1)
                link(v.scalar_tensor_tensor(got[1][:, t, :], got[1][:, t, :], wtok[:, 1, t:t + 1], got[0][:, t, :],
                                            ALU.mult, ALU.add))
                link(v.tensor_tensor(got[1][:, t, :], got[1][:, t, :], gbB[:, t // TB, :], ALU.mult))
                v.wait_ge(s["y_ok"], T)
                v.tensor_tensor(y[:, t, :], y[:, t, :], got[1][:, t, :], ALU.add).then_inc(s["y_ok"], 1)

        @block.tensor
        def _(pe):
            mm = pe.matmul
            pe.wait_ge(s["const"], 11)
            pe.wait_ge(s["silc"], 1)
            for k in range(KD):
                last = pe.transpose(bank[0][:, k * B:(k + 1) * B], sc_sb[:, k * P:(k + 1) * P], ident[0:B, 0:B])
            last.then_inc(s["cT"], 1)
            pe.wait_ge(s["d_gw"], 16)
            for k in range(KD):
                last = pe.transpose(bank[1][:, k * E:(k + 1) * E], gw_sb[:, k * P:(k + 1) * P], ident[0:E, 0:E])
            last.then_inc(s["gwT_ps"], 1)
            pe.wait_ge(s["scT_ok"], 1)
            pe.wait_ge(s["d_wmod"], 16)
            for m in range(4):
                for k in range(KD):
                    last = mm(bank[2][:, m * B:(m + 1) * B], wmod_sb[:, k, m * P:(m + 1) * P], scT[:, k, :],
                              start=(k == 0), stop=(k == KD - 1))
            last.then_inc(s["modT_ps"], 1)
            for i in range(2):
                for k in range(KD):
                    last = mm((bank[3], bank[0])[i][0:B, :], scT[:, k, :], wmod_sb[:, k, (i + 1) * 512:(i + 2) * 512],
                              start=(k == 0), stop=(k == KD - 1))
                last.then_inc(s["modrow_ps"], 1)
            for b in range(B):
                pe.wait_ge(s["xn_ok"], TB * (b + 1))
                for k in range(KD):
                    for t in range(TB):
                        last = pe.transpose(bank[4 + b][:, k * L + t * P:k * L + (t + 1) * P],
                                            xn[:, TB * b + t, k * P:(k + 1) * P], ident[:])
                last.then_inc(s["xT_ps"], 1)
            pe.wait_ge(s["d_wqkvu"], 64)
            pe.wait_ge(s["hT_a"], B)
            pe.wait_ge(s["hT_v"], B)
            pe.wait_ge(s["gwT_ok"], 1)
            pe.wait_ge(s["modrow_ok"], 1)
            for i in range(4):
                j, h = i // 2, i % 2
                for k in range(KD):
                    last = mm(bank[i][:], wqkvu[:, k, 0, j * P:(j + 1) * P], hT[:, k, h * 512:(h + 1) * 512],
                              start=(k == 0), stop=(k == KD - 1))
                last.then_inc(s["qT_ps"], 1)
            for t in range(T):
                if t >= 2:
                    pe.wait_ge(s["kvu_v"], 2 * (t - 1))
                    pe.wait_ge(s["kvu_a"], t - 1)
                for w, bk, n in ((1, 4, 2), (3, 5, 1)):
                    for k in range(KD):
                        last = mm(bank[bk + 2 * (t % 2)][:, 0:n * D], hT[:, k, t * P:(t + 1) * P],
                                  wqkvu[:, k, w:w + n, :].rearrange("p w d -> p (w d)"), start=(k == 0), stop=(k == KD - 1))
                last.then_inc(s["kvu_ps"], 1)
            pe.wait_ge(s["qT_a"], 2)
            pe.wait_ge(s["qT_v"], 2)
            for b in range(B):
                pe.wait_ge(s["kvu_v"], 2 * TB * (b + 1))
                for k in range(KD):
                    for t in range(TB):
                        last = mm(bank[b][:, k * P:(k + 1) * P], kvu[:, TB * b + t, 0, k * P:(k + 1) * P],
                                  kvu[:, TB * b + t, 1, k * P:(k + 1) * P], start=(t == 0), stop=(t == TB - 1))
                last.then_inc(s["kv_ps"], 1)
            pe.wait_ge(s["kvu_a"], T)
            for b in range(B):
                pe.wait_ge(s["kvm_ok"], b + 1)
                for t in range(TB):
                    for k in range(KD):
                        last = mm(bank[4 + b][:, t * D + k * P:t * D + (k + 1) * P], qT[:, k, (TB * b + t) * P:(TB * b + t + 1) * P],
                                  kvm[:, b, k, :], start=True, stop=True)
                last.then_inc(s["o_ps"], 1)
            pe.wait_ge(s["kvm_ok"], B)
            for i in range(2 * B):
                b, h = i // 2, i % 2
                if i >= 4:
                    pe.wait_ge(s["modB_ok"], i - 3)
                mm(bank[i % 4][:], sel[:, b, :], modrow[:, 2 * h:2 * h + 2, :].rearrange("b w d -> b (w d)"),
                   start=True, stop=True).then_inc(s["modB_ps"], 1)
            for b in range(B):
                pe.wait_ge(s["a_ok"], b + 1)
                for k in range(KD):
                    for t in range(TB):
                        last = pe.transpose(bank[4 + b][:, k * L + t * P:k * L + (t + 1) * P],
                                            ou[:, TB * b + t, k * P:(k + 1) * P], ident[:])
                last.then_inc(s["aT_ps"], 1)
            pe.wait_ge(s["d_wo"], 16)
            pe.wait_ge(s["modB_ok"], 2 * B)
            for b in range(B):
                pe.wait_ge(s["aT_v" if b % 2 else "aT_a"], b // 2 + 1)
                for t in range(TB):
                    for k in range(KD):
                        last = mm(bank[b][:, t * D:(t + 1) * D], aT[:, k, (TB * b + t) * P:(TB * b + t + 1) * P], wo_sb[:, k, :],
                                  start=(k == 0), stop=(k == KD - 1))
                last.then_inc(s["wo_ps"], 1)
            for b in range(B):
                pe.wait_ge(s["h2_ok"], TB * (b + 1))
                for k in range(KD):
                    for t in range(TB):
                        last = pe.transpose(bank[4 + b][:, k * L + t * P:k * L + (t + 1) * P],
                                            xn[:, TB * b + t, k * P:(k + 1) * P], ident[:])
                last.then_inc(s["h2T_ps"], 1)
            pe.wait_ge(s["lgT_ok"], B)
            for t in range(T):
                for k in range(KD):
                    last = mm(bank[0][:, t * E:(t + 1) * E], hT[:, k, t * P:(t + 1) * P], gwT[:, k, :],
                              start=(k == 0), stop=(k == KD - 1))
            last.then_inc(s["lg_ps"], 1)
            pe.wait_ge(s["mask_ok"], 1)
            mask = lg[:, 6].rearrange("p t e -> p (t e)")
            mm(bank[0][:, T * E:2 * T * E], triu[:], mask, start=True, stop=True)
            mm(bank[0][:, 2 * T * E:3 * T * E], ones[:], mask, start=True, stop=True).then_inc(s["rank_ps"], 1)
            pe.wait_ge(s["h2lo"], B)
            pe.wait_ge(s["pos_ok"], 1)

            def gate_up(st, part, x_hi, x_lo, off, first):
                if not first:
                    pe.wait_ge(s["mul_ok"], 2 * st + part - 1)
                outs = ((GATE, bank[0][:]), (UP, bank[1][:])) if part == 0 else \
                       ((GATE, bank[2][:, 0:FB]), (UP, bank[2][:, FB:2 * FB]))
                c0, n = (0, FA) if part == 0 else (FA, FB)
                for k in range(KD):
                    for x_, ws in ((x_hi, (whi, wlo)), (x_lo, (whi,))):
                        for w, o in outs:
                            for W in ws:
                                start = k == 0 and x_ is x_hi and W is whi and (part == 0 or w == GATE)
                                last = mm(o, x_[:, k, :], gu_at(W, off, k, w, c0, n), start=start,
                                          stop=(k == KD - 1 and x_ is x_lo), skip_group_check=True)
                last.then_inc(s["gu_ps"], 1)

            def turn(st, par, first):
                pe.wait_ge(s["mul_ok"], 2 * st + 2)
                if not first:
                    pe.wait_ge(s["tlo"], 2 * st)
                for ch in range(FC):
                    last = pe.transpose(bank[4 + ch // 4][0:FR[ch], (ch % 4) * P:(ch % 4 + 1) * P],
                                        actv[:, par, FO[ch]:FO[ch] + FR[ch]], ident[:])
                last.then_inc(s["t_ps"], 1)

            def down(st, par, off, free):
                pe.wait_ge(s["tlo"], 2 * st + 2)
                for name, n in free:
                    pe.wait_ge(s[name], n)
                for ch in range(FC):
                    r = FR[ch]
                    for i, (a_, W) in enumerate(((aThi, whi), (aThi, wlo), (aTlo, whi))):
                        last = mm(bank[6 + par][:, 0:D], a_[0:r, ch, :], down_at(W, off, ch),
                                  start=(ch == 0 and i == 0), stop=(ch == FC - 1 and i == 2))
                last.then_inc(s["y_ps"], 1)

            def rows(i, par, count, free):
                pe.wait_ge(d_xg[par], count)
                if free is not None:
                    pe.wait_ge(s["xlo"], free)
                for k in range(KD):
                    last = pe.transpose(bank[3][:, k * P:(k + 1) * P], xg[:, par, k * P:(k + 1) * P], ident[:])
                last.then_inc(s["x_ps"], 1)

            def bank_read(st):
                r = st - 2
                if r < 0:
                    return []
                if r < SA:
                    return [("y_ok", r + 1)]
                if r < SA + NR:
                    return [("ycopy", r - SA + 1)]
                return [("y_ok", r - NR + 1)]

            def shared(st, off, prev_off):
                par, t = st % 2, st if st < SA else st - NR
                xh, xl = hThi[:, :, t * P:(t + 1) * P], hTlo[:, :, t * P:(t + 1) * P]
                gate_up(st, 0, xh, xl, off, st == 0)
                if st:
                    turn(st - 1, 1 - par, st == 1)
                gate_up(st, 1, xh, xl, off, st == 0)
                if st:
                    down(st - 1, 1 - par, prev_off, bank_read(st - 1))

            def offset(i):
                return pe.value_load(tab[0:1, 0, bass.ds(i, 1)], min_val=0, max_val=W1)

            def routed(i, par, prev_off, free, next_count):
                st = i + SA
                loads = pe.value_load(tab[0:1, 1, bass.ds(i, 1)], min_val=2, max_val=E + 1)
                off = offset(i)
                pe.wait_ge(s["split"], loads)
                pe.wait_ge(s["xlo"], i + 1)
                gate_up(st, 0, xThi[:, par], xTlo[:, par], off, False)
                turn(st - 1, 1 - par, False)
                gate_up(st, 1, xThi[:, par], xTlo[:, par], off, False)
                if next_count is not None:
                    rows(i + 1, 1 - par, next_count, i + 1)
                down(st - 1, 1 - par, offset(i - 1) if prev_off is None else prev_off, free)

            pe.wait_ge(s["split"], 1)
            for st in range(SA):
                shared(st, 0, 0)
            rows(0, 0, 16, None)
            pe.wait_ge(s["tab_ok"], 1)
            for i in range(3):
                routed(i, i % 2, None if i else 0, bank_read(SA + i - 1), 16 * ((i + 1) // 2 + 1))
            pairs = (NR - 5) // 2
            with pe.Fori(0, pairs) as j:
                routed(2 * j + 3, 1, None, [("ycopy", 2 * j + 1)], 16 * j + 48)
                routed(2 * j + 4, 0, None, [("ycopy", 2 * j + 2)], 16 * j + 48)
            for i in range(2 * pairs + 3, NR):
                routed(i, i % 2, None, bank_read(SA + i - 1), 16 * ((i + 1) // 2 + 1) if i + 1 < NR else None)
            pe.wait_ge(s["split"], NX)
            last_off = ((NX - 1) % 2) * W1
            for st in range(SA + NR, NS):
                shared(st, last_off, offset(NR - 1) if st == SA + NR else last_off)
            turn(NS - 1, (NS - 1) % 2, False)
            down(NS - 1, (NS - 1) % 2, last_off, bank_read(NS - 1))


_INS = ['L0_attn_x', 'L0_attn_Wq', 'L0_attn_Wk', 'L0_attn_Wv', 'L0_attn_Wu', 'L0_attn_Wo', 'L0_ffn_gate_w',
        'L0_ffn_w_gate', 'L0_ffn_w_up', 'L0_ffn_w_down', 'L0_ffn_sw_gate', 'L0_ffn_sw_up', 'L0_ffn_sw_down',
        'L0_c', 'L0_wmod']


def kernel(**inputs):
    import numpy as _np
    import concourse.bacc as _bacc
    from concourse import mybir as _mybir
    from concourse.bass_utils import run_bass_kernel_spmd as _run

    nc = _bacc.Bacc("TRN2", target_bir_lowering=False, num_devices=1)
    arrays, args = {}, []
    for name in _INS:
        a = _np.ascontiguousarray(inputs[name])
        arrays[f"in_{name}_dram"] = a
        args.append(nc.dram_tensor(f"in_{name}_dram", a.shape, _mybir.dt.from_np(a.dtype), kind="ExternalInput").ap())
    out = nc.dram_tensor("out_0_dram", inputs['L0_attn_x'].shape, _mybir.dt.float32, kind="ExternalOutput").ap()
    adaln_block(nc, *args, out)
    r = _run(nc, [arrays], core_ids=[0])
    return r.results[0]["out_0_dram"]
```
